# Optimizing a Trainium2 kernel written in Bass

```python
import numpy as np
import jax
import jax.numpy as jnp

def _softmax(x, axis=-1):
    return jax.nn.softmax(x, axis=axis)

def _gelu(x):
    return jax.nn.gelu(x, approximate=True)

def _silu(x):
    return jax.nn.silu(x)

def _sigmoid(x):
    return jax.nn.sigmoid(x)

def _layernorm(x, axis=-1, eps=1e-05):
    m = jnp.mean(x, axis=axis, keepdims=True)
    v = jnp.var(x, axis=axis, keepdims=True)
    return (x - m) / jnp.sqrt(v + eps)

def _scatter_add(tgt, idx, src, axis=0):
    return tgt.at[idx].add(src)

def _segment_sum(src, seg, n):
    return jax.ops.segment_sum(src, seg, n)
kernel_name = 'mk_adj_preln_d4_adj_r2_d3ab20'

def setup_inputs(seed: int=0):
    np.random.seed(seed)
    _w = jnp.asarray

    def _rec_inputs():
        import jax
        import jax.numpy as jnp
        _gk = jax.random.key(seed)
        x = -0.0002928 + 1 * jax.random.normal(jax.random.fold_in(_gk, 1), (16, 512, 128), jnp.float32)
        _a = jax.random.bernoulli(jax.random.fold_in(_gk, 2), 0.0078125, (16, 512, 512))
        _a = jnp.logical_or(_a, jnp.swapaxes(_a, -1, -2))
        _a = jnp.logical_or(_a, jnp.eye(512, dtype=bool))
        _af = _a.astype(jnp.float32)
        _af = _af * jax.random.uniform(jax.random.fold_in(_gk, 3), (16, 512, 512), jnp.float32, 0.05, 1)
        adj = _af
        _nm = jnp.ones((16, 512), dtype=bool)
        nodemask = jnp.where(_nm, 1.0, 0.0).astype(jnp.float32)
        return (x, adj, nodemask)
    x, adj, nodemask = _rec_inputs()

    def _L0_gnn_setup():
        import jax, jax.numpy as jnp
        import numpy as np
        B, N, DIN = (16, 512, 128)
        HEADS, OUT_DIM = (4, 128)
        F = OUT_DIM // HEADS
        NEG_SLOPE = 0.2
        MASK_VAL = -1000000000.0
        key = jax.random.key(seed)
        k1, k2, k3, k4, k5, k6 = jax.random.split(key, 6)
        x = jax.random.normal(k1, (B, N, DIN), dtype=jnp.float32)
        adj = jax.random.uniform(k2, (B, N, N), dtype=jnp.float32)
        W = jax.random.normal(k3, (DIN, HEADS, F), dtype=jnp.float32) * (1.0 / np.sqrt(DIN))
        a_src = jax.random.normal(k4, (HEADS, F), dtype=jnp.float32) * (1.0 / np.sqrt(F))
        a_dst = jax.random.normal(k5, (HEADS, F), dtype=jnp.float32) * (1.0 / np.sqrt(F))
        bias = jax.random.normal(k6, (OUT_DIM,), dtype=jnp.float32) * 0.01
        return {'x': x, 'adj': adj, 'W': W, 'a_src': a_src, 'a_dst': a_dst, 'bias': bias}
    _L0_gnn_all = _L0_gnn_setup()
    _L0_gnn_in = {k: v for k, v in _L0_gnn_all.items() if k in ('W', 'a_src', 'a_dst', 'bias')}
    del _L0_gnn_all

    def _L1_gnn_setup():
        import jax, jax.numpy as jnp
        import numpy as np
        B, N, F = (8, 512, 128)
        OUT, REL = (128, 16)
        NADJ = 7
        key = jax.random.key(seed)
        k0, k1, k2, k3, k4 = jax.random.split(key, 5)
        features = jax.random.normal(k0, (B, N, F), dtype=jnp.float32)
        A1 = jax.random.uniform(k1, (B, N, N), dtype=jnp.float32)
        A2 = jax.random.uniform(k2, (B, N, N), dtype=jnp.float32)
        W = jax.random.normal(k3, (NADJ, F + REL, OUT), dtype=jnp.float32) * 0.05
        W_edges = jnp.ones((NADJ, REL), dtype=jnp.float32)
        b = jax.random.uniform(k4, (N, OUT), dtype=jnp.float32, minval=-0.05, maxval=0.05)
        return {'features': features, 'A1': A1, 'A2': A2, 'W': W, 'W_edges': W_edges, 'b': b}
    _L1_gnn_all = _L1_gnn_setup()
    _L1_gnn_in = {k: v for k, v in _L1_gnn_all.items() if k in ('W', 'W_edges', 'b')}
    del _L1_gnn_all

    def _L2_gnn_setup():
        import jax, jax.numpy as jnp
        import numpy as np
        EPS = 1e-08
        key = jax.random.key(seed)
        kH, kA, kW = jax.random.split(key, 3)
        B, N, IN, OUT = (32, 256, 128, 128)
        H = jax.random.normal(kH, (B, N, IN), dtype=jnp.float32)
        A = jax.random.uniform(kA, (B, N, N), dtype=jnp.float32)
        mask = jnp.ones((B, N), dtype=jnp.float32)
        W = jax.random.normal(kW, (OUT, IN), dtype=jnp.float32) * (1.0 / np.sqrt(IN))
        b = jnp.zeros((OUT,), dtype=jnp.float32)
        return {'H': H, 'A': A, 'mask': mask, 'W': W, 'b': b}
    _L2_gnn_all = _L2_gnn_setup()
    _L2_gnn_in = {k: v for k, v in _L2_gnn_all.items() if k in ('W', 'b')}
    del _L2_gnn_all

    def _L3_gnn_setup():
        import jax, jax.numpy as jnp
        import numpy as np
        LN_EPS = 1e-05
        key = jax.random.key(seed)
        k1, k2, k3, k4 = jax.random.split(key, 4)
        B, N, F, O = (8, 1024, 128, 128)
        x = jax.random.normal(k1, (B, N, F), dtype=jnp.float32)
        adj = jax.random.uniform(k2, (B, N, N), dtype=jnp.float32)
        gamma = jnp.ones((F,), jnp.float32)
        beta = jnp.zeros((F,), jnp.float32)
        W_self = jax.random.normal(k3, (F, O), dtype=jnp.float32) * (1.0 / np.sqrt(F))
        W_neigh = jax.random.normal(k4, (F, O), dtype=jnp.float32) * (1.0 / np.sqrt(F))
        return {'x': x, 'adj': adj, 'gamma': gamma, 'beta': beta, 'W_self': W_self, 'W_neigh': W_neigh}
    _L3_gnn_all = _L3_gnn_setup()
    _L3_gnn_in = {k: v for k, v in _L3_gnn_all.items() if k in ('gamma', 'beta', 'W_self', 'W_neigh')}
    del _L3_gnn_all
    return {'x': x, 'adj': adj, 'nodemask': nodemask, 'L0_gnn_W': _L0_gnn_in['W'], 'L0_gnn_a_src': _L0_gnn_in['a_src'], 'L0_gnn_a_dst': _L0_gnn_in['a_dst'], 'L0_gnn_bias': _L0_gnn_in['bias'], 'L1_gnn_W': _L1_gnn_in['W'], 'L1_gnn_W_edges': _L1_gnn_in['W_edges'], 'L1_gnn_b': _L1_gnn_in['b'], 'L2_gnn_W': _L2_gnn_in['W'], 'L2_gnn_b': _L2_gnn_in['b'], 'L3_gnn_gamma': _L3_gnn_in['gamma'], 'L3_gnn_beta': _L3_gnn_in['beta'], 'L3_gnn_W_self': _L3_gnn_in['W_self'], 'L3_gnn_W_neigh': _L3_gnn_in['W_neigh']}

def reference(x, adj, nodemask, L0_gnn_W, L0_gnn_a_src, L0_gnn_a_dst, L0_gnn_bias, L1_gnn_W, L1_gnn_W_edges, L1_gnn_b, L2_gnn_W, L2_gnn_b, L3_gnn_gamma, L3_gnn_beta, L3_gnn_W_self, L3_gnn_W_neigh):
    import jax
    import jax.numpy as jnp

    def _L0_gnn_ref(x, adj, W, a_src, a_dst, bias):
        import jax, jax.numpy as jnp
        import numpy as np
        B, N, DIN = (16, 512, 128)
        HEADS, OUT_DIM = (4, 128)
        F = OUT_DIM // HEADS
        NEG_SLOPE = 0.2
        MASK_VAL = -1000000000.0
        b, n, _ = x.shape
        h = jnp.einsum('bnd,dhf->bnhf', x, W)
        e_src = jnp.einsum('bnhf,hf->bhn', h, a_src)
        e_dst = jnp.einsum('bnhf,hf->bhn', h, a_dst)
        e = e_dst[:, :, :, None] + e_src[:, :, None, :]
        e = jax.nn.leaky_relu(e, NEG_SLOPE)
        mask = (adj > 0.5)[:, None, :, :]
        e = jnp.where(mask, e, MASK_VAL)
        attn = jax.nn.softmax(e, axis=-1)
        out = jnp.einsum('bhij,bjhf->bihf', attn, h)
        out = out.reshape(b, n, HEADS * F) + bias
        return out

    def _L1_gnn_ref(features, A1, A2, W, W_edges, b):
        import jax, jax.numpy as jnp
        import numpy as np
        B, N, F = (8, 512, 128)
        OUT, REL = (128, 16)
        NADJ = 7
        eye = jnp.zeros_like(A1) + jnp.eye(N, dtype=A1.dtype)
        shifted = jnp.roll(eye, 1, axis=0)
        A_fwd = [A1, A2, shifted]
        A_list = A_fwd + [jnp.swapaxes(a, 1, 2) for a in A_fwd]
        A_list.append(eye)
        A = jnp.stack(A_list, axis=0)
        HW = jnp.einsum('bnf,rfo->rbno', features, W[:, :F]) + jnp.einsum('rd,rdo->ro', W_edges, W[:, F:])[:, None, None, :]
        AHW = jnp.einsum('rbnm,rbmo->rbno', A, HW)
        out = jnp.max(AHW, axis=0) + b
        return out

    def _L2_gnn_ref(H, A, mask, W, b):
        import jax, jax.numpy as jnp
        import numpy as np
        EPS = 1e-08
        N = A.shape[-1]
        A_hat = A + jnp.eye(N, dtype=A.dtype)
        deg = A_hat.sum(axis=-1)
        dis = (deg + EPS) ** (-0.5)
        A_norm = dis[:, :, None] * A_hat * dis[:, None, :]
        H_lin = jnp.einsum('bni,oi->bno', H, W) + b
        out = jnp.einsum('bnm,bmo->bno', A_norm, H_lin)
        out = out * mask[:, :, None]
        return jax.nn.relu(out)

    def _L3_gnn_ref(x, adj, gamma, beta, W_self, W_neigh):
        import jax, jax.numpy as jnp
        import numpy as np
        LN_EPS = 1e-05
        mu = jnp.mean(x, axis=-1, keepdims=True)
        var = jnp.mean(jnp.square(x - mu), axis=-1, keepdims=True)
        xn = (x - mu) * jax.lax.rsqrt(var + LN_EPS) * gamma + beta
        d_out = jnp.sum(adj, axis=1)
        d_in = jnp.sum(adj, axis=2)
        s_out = jnp.where(d_out != 0, jax.lax.rsqrt(d_out), 0.0)
        s_in = jnp.where(d_in != 0, jax.lax.rsqrt(d_in), 0.0)
        A_norm = s_out[:, :, None] * adj * s_in[:, None, :]
        eye = jnp.eye(adj.shape[1], dtype=adj.dtype)
        L = eye[None, :, :] - A_norm
        neighbor = jnp.einsum('bij,bjf->bif', L, xn)
        pre = xn @ W_self + neighbor @ W_neigh
        return jax.nn.softplus(pre)
    h = jnp.maximum(_layernorm(x, axis=-1), 0.0)
    x = x + _L0_gnn_ref(h, adj, L0_gnn_W, L0_gnn_a_src, L0_gnn_a_dst, L0_gnn_bias)
    h = jnp.maximum(_layernorm(x, axis=-1), 0.0)
    x = x + _L1_gnn_ref(h, adj, adj, L1_gnn_W, L1_gnn_W_edges, L1_gnn_b)
    h = jnp.maximum(_layernorm(x, axis=-1), 0.0)
    x = x + _L2_gnn_ref(h, adj, nodemask, L2_gnn_W, L2_gnn_b)
    h = jnp.maximum(_layernorm(x, axis=-1), 0.0)
    x = x + _L3_gnn_ref(h, adj, L3_gnn_gamma, L3_gnn_beta, L3_gnn_W_self, L3_gnn_W_neigh)
    return x

_drawn_inputs = setup_inputs


def setup_inputs(seed=0):
    import zlib

    import numpy as np

    out = dict(_drawn_inputs(seed))
    spreads = {'L1_gnn_W_edges': (1.0, 0.2),
     'L2_gnn_b': (0.0, 0.296),
     'L3_gnn_gamma': (1.0, 0.2),
     'L3_gnn_beta': (0.0, 0.487)}
    factors = {'L0_gnn_a_dst': 16.301, 'L0_gnn_bias': 8.0, 'L1_gnn_b': 5.773}
    for name, (base, spread) in spreads.items():
        noise = np.random.default_rng([zlib.crc32(name.encode()), seed]).standard_normal(out[name].shape)
        drawn = base * np.exp(spread * noise) if base else spread * noise
        out[name] = jnp.asarray(drawn.astype(out[name].dtype))
    for name, factor in factors.items():
        out[name] = (out[name] * factor).astype(out[name].dtype)
    return out
```

```python
from contextlib import ExitStack

import concourse.bass as bass
from concourse import mybir

fp32 = mybir.dt.float32
f32r = mybir.dt.float32r
bf16 = mybir.dt.bfloat16
ALU = mybir.AluOpType
ACT = mybir.ActivationFunctionType
AX = mybir.AxisListType
RMAX = bass.bass_isa.ReduceOp.max

GRAPHS, N, F = 16, 512, 128
P = 128
T = N // P
HEADS = 4
HF = F // HEADS
GRP = HF + 1
VAL = 2 * GRP
RELS, REL = 7, 16
ORDER = (0, 1, 3, 4, 2, 5, 6)
PARTS = 3
LN_EPS, DEG_EPS = 1e-5, 1e-8
SLOPE, SHIFT, EDGE = 0.2, 64.0, 0.5
ACT_SET = "natural_log_exp_and_others"


class Graph:

    def __init__(self, off, it=None):
        self.off, self.it, self.par = off, it, off % 2

    def number(self):
        return self.off if self.it is None else self.it * 2 + self.off

    def th(self, k, per):
        rest = per * self.off + k
        return rest if self.it is None else self.it * (2 * per) + rest

    def all(self, per):
        return self.th(per, per)

    def loaded(self):
        rest = 16 * (self.off // 2 + 1)
        return rest if self.it is None else self.it * 16 + rest

    def has(self, n):
        return self.it is not None or self.off >= n

    def before(self, n):
        return Graph(self.off - n, self.it)


def of_graph(piece):
    return lambda g: None if g is None else piece(g)


def graph_kernel(nc, x, adj, nodemask, w0, a_src, a_dst, bias0, w1, w_edges, b1, w2, b2,
                 gamma, beta, w_self, w_neigh, out):
    ctx = ExitStack()
    with ctx:
        def sb(name, shape, dt=fp32):
            return ctx.enter_context(nc.sbuf_tensor(name, shape, dt))

        def sem(name):
            return ctx.enter_context(nc.semaphore(name))

        ident = sb("ident", [P, P])
        half_neg = sb("half_neg", [P, 3 * T])
        shift_c = sb("shift_c", [P, 1])
        mean_w = sb("mean_w", [P, P])
        w0c = sb("w0c", [P, F + 2 * HEADS])
        a_bc = sb("a_bc", [P, 2, F])
        wa_tmp = sb("wa_tmp", [P, 2, F])
        bias0_bc = sb("bias0_bc", [P, F])
        b2_bc = sb("b2_bc", [P, F])
        gamma_bc = sb("gamma_bc", [P, F])
        beta_bc = sb("beta_bc", [P, F])
        b1_sb = sb("b1_sb", [P, T, F])
        w1_sb = sb("w1_sb", [P, RELS, F])
        w1_edge = sb("w1_edge", [REL, RELS, F])
        edge_t = sb("edge_t", [REL, RELS])
        c_row = sb("c_row", [1, RELS, F])
        c_split = sb("c_split", [1, 2, RELS * F], f32r)
        c_rows = sb("c_rows", [8, RELS * F], f32r)
        w2_in = sb("w2_in", [P, F])
        w2_t = sb("w2_t", [P, F])
        w3_self = sb("w3_self", [P, F])
        w3_neigh = sb("w3_neigh", [P, F])
        w3_sum = sb("w3_sum", [P, F])
        mask_in = sb("mask_in", [GRAPHS * T, P])
        mask_t = sb("mask_t", [P, GRAPHS, T])

        adj_in = [sb(f"adj_in{i}", [P, T, N]) for i in range(2)]
        adj_tr = [sb(f"adj_tr{i}", [P, T, N]) for i in range(2)]
        x_in = [sb(f"x_in{i}", [P, T, F]) for i in range(2)]
        x1 = [sb(f"x1_{i}", [P, T, F]) for i in range(2)]
        y_out = sb("y_out", [P, T, F])
        sums = [sb(f"sums{i}", [P, 2, T]) for i in range(2)]
        deg = [sb(f"deg{i}", [P, 3, T]) for i in range(2)]
        zero_deg = [sb(f"zero_deg{i}", [P, 2, T]) for i in range(2)]
        deg_pow = [sb(f"deg_pow{i}", [P, 3, T]) for i in range(2)]
        scales = [sb(f"scales{i}", [P, 4, T]) for i in range(2)]
        sum_cols = [sb(f"sum_cols{i}", [P, T, 8], f32r) for i in range(2)]

        junk = sb("junk", [P, T, N], bf16)
        xb = [sb(f"xb{i}", [P, T, F]) for i in range(2)]
        st0 = sb("st0", [P, T, 6])
        mv0 = sb("mv0", [P, T, 2])
        ve0 = sb("ve0", [P, T])
        rstd0 = sb("rstd0", [P, T])
        g0 = sb("g0", [P, T, F])
        h0 = sb("h0", [P, T, F])
        h0t = sb("h0t", [P, N])
        mask = sb("mask", [P, T, N], bf16)
        nmask = sb("nmask", [P, T, N], bf16)
        hv = sb("hv", [P, T, F])
        sd = sb("sd", [P, T, 2, HEADS])
        smax_p = sb("smax_p", [P, HEADS])
        smax = sb("smax", [P, HEADS])
        neg_s = sb("neg_s", [P, T, HEADS])
        s_rel = sb("s_rel", [P, T, HEADS])
        d_top = sb("d_top", [P, T, HEADS])
        d_low = sb("d_low", [P, T, HEADS])
        b12 = sb("b12", [P, T, HEADS, 2])
        a2 = sb("a2", [P, T, HEADS])
        val = sb("val", [P, T, HEADS, VAL])
        rest = sb("rest", [P, T, HEADS, VAL])
        parts = [sb(f"part{i}", [P, T, HEADS, VAL], bf16) for i in range(PARTS)]
        pos = [sb(f"pos{i}", [P, T, N], bf16) for i in range(2)]
        low = sb("low", [P, T, 2, GRP])
        num = sb("num", [P, T, HEADS, GRP])
        empty = sb("empty", [P, T, HEADS])
        den = sb("den", [P, T, HEADS])
        rden = sb("rden", [P, T, HEADS])
        att = sb("att", [P, T, F])
        xe = sb("xe", [P, T, F])
        xf = sb("xf", [P, T, F])

        stl = sb("stl", [P, T, 6])
        mvl = sb("mvl", [P, T, 2])
        vel = sb("vel", [P, T])
        rstdl = sb("rstdl", [P, T])
        gl = sb("gl", [P, T, F])
        h1 = sb("h1", [P, T, F])
        h1t = sb("h1t", [P, N])
        aht = sb("aht", [P, N])
        atht = sb("atht", [P, N])
        sum_rows = sb("sum_rows", [8, N], f32r)
        x1b = sb("x1b", [P, T, F])
        best = sb("best", [P, T, F])
        x2 = sb("x2", [P, T, F])
        h2 = sb("h2", [P, T, F])
        h2t = sb("h2t", [P, N])
        lin2 = sb("lin2", [P, T, F])
        y2 = sb("y2", [P, T, F])
        ay2t = sb("ay2t", [P, N])
        r2 = sb("r2", [P, T, F])
        x3 = sb("x3", [P, T, F])
        mv4 = sb("mv4", [P, T, 2])
        ve4 = sb("ve4", [P, T])
        xg = sb("xg", [P, T, F])
        xn = sb("xn", [P, T, F])
        xnt = sb("xnt", [P, N])
        z3 = sb("z3", [P, T, F])
        g3t = sb("g3t", [P, N])
        p2 = sb("p2", [P, T, F])
        pre = sb("pre", [P, T, F])
        mag = sb("mag", [P, T, F])
        ex = sb("ex", [P, T, F])
        lg = sb("lg", [P, T, F])
        sp = sb("sp", [P, T, F])

        early_t = [ctx.enter_context(nc.psum_tensor(f"early_t{i}", [P, N], fp32)) for i in range(2)]
        early_a = ctx.enter_context(nc.psum_tensor("early_a", [P, 2, 512], fp32))
        late_a = [ctx.enter_context(nc.psum_tensor(f"late_a{i}", [P, 2, 512], fp32)) for i in range(2)]
        bank = [late_a[0][:, 0, :], late_a[0][:, 1, :], late_a[1][:, 0, :], late_a[1][:, 1, :]]

        gate_dve = sem("gate_dve")
        gate_pool = sem("gate_pool")
        s_const = sem("s_const")
        s_adj = [sem(f"s_adj{i}") for i in range(2)]
        s_x = [sem(f"s_x{i}") for i in range(2)]
        s_store = sem("s_store")
        s_pool = sem("s_pool")
        s_setup = sem("s_setup")
        s_setup_pe = sem("s_setup_pe")
        s_rows = sem("s_rows")

        adj_ps = sem("adj_ps")
        adj_sb = sem("adj_sb")
        row_sum = sem("row_sum")
        edges = sem("edges")
        nedges = sem("nedges")
        deg_in = sem("deg_in")
        deg_out = sem("deg_out")
        deg_ok = sem("deg_ok")
        cols_ok = sem("cols_ok")
        xb_ok = sem("xb_ok")
        bn0 = sem("bn0")
        pow0 = sem("pow0")
        cen0 = sem("cen0")
        h0_ok = sem("h0_ok")
        h0t_ps = sem("h0t_ps")
        h0t_sb = sem("h0t_sb")
        proj_ps = sem("proj_ps")
        hv_ok = sem("hv_ok")
        sd_ok = sem("sd_ok")
        negs_ok = sem("negs_ok")
        smaxp_ok = sem("smaxp_ok")
        smax_ok = sem("smax_ok")
        rel_ok = sem("rel_ok")
        b_ok = sem("b_ok")
        val_ok = sem("val_ok")
        valc_ok = sem("valc_ok")
        hi_ok = sem("hi_ok")
        rest_ok = sem("rest_ok")
        mid_ok = sem("mid_ok")
        lo_ok = sem("lo_ok")
        dbc_ps = sem("dbc_ps")
        pos_ok = sem("pos_ok")
        pos_used = sem("pos_used")
        low_ok = sem("low_ok")
        num_ok = sem("num_ok")
        mean_ps = sem("mean_ps")
        end0 = sem("end0")

        bnl = sem("bnl")
        powl = sem("powl")
        cenl = sem("cenl")
        hl = sem("hl")
        sums_ps = sem("sums_ps")
        sums_sb = sem("sums_sb")
        h1t_ps = sem("h1t_ps")
        h1t_sb = sem("h1t_sb")
        hw_ps = sem("hw_ps")
        best_ok = sem("best_ok")
        x1b_ok = sem("x1b_ok")
        x2_ok = sem("x2_ok")
        h2t_ps = sem("h2t_ps")
        h2t_sb = sem("h2t_sb")
        lin2_ps = sem("lin2_ps")
        lin2_ok = sem("lin2_ok")
        y2_ok = sem("y2_ok")
        ay2_ps = sem("ay2_ps")
        ay2_sb = sem("ay2_sb")
        back_ps = sem("back_ps")
        r2_ok = sem("r2_ok")
        x3_ok = sem("x3_ok")
        xg_ok = sem("xg_ok")
        xn_ok = sem("xn_ok")
        xnt_ps = sem("xnt_ps")
        xnt_sb = sem("xnt_sb")
        z3_ok = sem("z3_ok")
        g3_ps = sem("g3_ps")
        g3_sb = sem("g3_sb")
        p3_ps = sem("p3_ps")
        p2_ok = sem("p2_ok")
        pre_ok = sem("pre_ok")
        soft = sem("soft")
        sp_ok = sem("sp_ok")
        y_ok = sem("y_ok")

        CONST_LOADS = 13 + RELS
        block = ctx.enter_context(nc.Block())

        def run_steps(eng, step):
            step(None, None, Graph(0))
            step(None, Graph(0), Graph(1))
            with eng.Fori(0, (GRAPHS - 2) // 2) as it:
                for u in range(2):
                    step(Graph(u, it), Graph(1 + u, it), Graph(2 + u, it))
            step(Graph(GRAPHS - 2), Graph(GRAPHS - 1), None)
            step(Graph(GRAPHS - 1), None, None)

        @block.sync
        def _(sync):
            def load(g):
                if g.has(2):
                    sync.wait_ge(h1t_ps, g.before(2).th(3, 3))
                sync.dma_start(adj_in[g.par][:, :, :], adj[bass.ts(g.number(), 1), :, :].rearrange(
                    "g (t p) m -> p (g t) m", p=P)).then_inc(s_adj[g.par], 16)
                if g.has(2):
                    sync.wait_ge(xb_ok, g.before(2).all(1))
                if g.has(2):
                    sync.wait_ge(cen0, g.before(2).all(1))
                sync.dma_start(x_in[g.par][:, :, :], x[bass.ts(g.number(), 1), :, :].rearrange(
                    "g (t p) f -> p (g t) f", p=P)).then_inc(s_x[g.par], 16)

            def store(g):
                sync.wait_ge(y_ok, g.all(1))
                sync.dma_start(out[bass.ts(g.number(), 1), :, :].rearrange(
                    "g (t p) f -> p (g t) f", p=P), y_out[:, :, :]).then_inc(s_store, 16)

            load(Graph(0))
            load(Graph(1))
            with nc.sync.Fori(0, (GRAPHS - 2) // 2) as it:
                for u in range(2):
                    load(Graph(2 + u, it))
                    store(Graph(u, it))
            store(Graph(GRAPHS - 2))
            store(Graph(GRAPHS - 1))
            sync.wait_ge(s_store, 16 * GRAPHS)

        @block.gpsimd
        def _(pool):
            nc.gpsimd.memset(ident[:], 0.0).then_inc(s_pool, 1)
            pool.wait_ge(s_pool, 1)
            nc.gpsimd.affine_select(out=ident[:], in_=ident[:], compare_op=ALU.not_equal, fill=1.0,
                                    base=0, pattern=[[-1, P]], channel_multiplier=1).then_inc(s_pool, 1)
            nc.gpsimd.memset(half_neg[:], -0.5).then_inc(s_pool, 1)
            pool.wait_ge(s_pool, 3)

            @of_graph
            def add_bias(g):
                pool.wait_ge(s_x[g.par], g.loaded())
                if g.has(2):
                    pool.wait_ge(end0, g.before(2).all(7))
                nc.gpsimd.tensor_tensor(xb[g.par][:], x_in[g.par][:], bias0_bc[:].unsqueeze(1).broadcast_to([P, T, F]),
                                        ALU.add).then_inc(xb_ok, 1)

            @of_graph
            def rstd_0(g):
                pool.wait_ge(bn0, g.all(3))
                nc.gpsimd.tensor_tensor(rstd0[:], ve0[:], half_neg[:, 0:T], ALU.pow).then_inc(pow0, 1)

            @of_graph
            def degrees(g):
                pool.wait_ge(deg_in, g.all(3))
                nc.gpsimd.tensor_tensor(deg_pow[g.par][:].rearrange("p a t -> p (a t)"),
                                        deg[g.par][:].rearrange("p a t -> p (a t)"),
                                        half_neg[:], ALU.pow).then_inc(deg_out, 1)

            @of_graph
            def values(g):
                pool.wait_ge(smaxp_ok, g.all(1))
                pool.sem_inc(gate_pool, 1)
                nc.gpsimd.partition_all_reduce(smax[:], smax_p[:], P, RMAX).then_inc(smax_ok, 1)
                pool.wait_ge(b_ok, g.th(1, 2))
                pool.wait_ge(hv_ok, g.all(1))
                if g.has(1):
                    pool.wait_ge(lo_ok, g.before(1).all(1))
                if g.has(1):
                    pool.wait_ge(rest_ok, g.before(1).th(1, 1))
                for k in range(2):
                    last = nc.gpsimd.tensor_tensor(
                        val[:, :, :, k * GRP:k * GRP + HF],
                        hv[:].rearrange("p t (h f) -> p t h f", h=HEADS),
                        b12[:, :, :, k:k + 1].broadcast_to([P, T, HEADS, HF]), ALU.mult)
                last.then_inc(val_ok, 1)

            def rstd(k):
                @of_graph
                def piece(g):
                    pool.wait_ge(bnl, g.th(12 if k == 3 else 3 * k, 12))
                    nc.gpsimd.tensor_tensor(rstdl[:], (ve4 if k == 3 else vel)[:], half_neg[:, 0:T], ALU.pow).then_inc(powl, 1)
                return piece

            @of_graph
            def add_b1(g):
                pool.wait_ge(end0, g.all(7))
                if g.has(1):
                    pool.wait_ge(x2_ok, g.before(1).all(1))
                nc.gpsimd.tensor_tensor(x1b[:], x1[g.par][:], b1_sb[:], ALU.add).then_inc(x1b_ok, 1)

            pool.wait_ge(s_const, 16 * CONST_LOADS)

            def step(p, g, n):
                rstd_0(n)
                add_bias(n)
                add_b1(g)
                values(n)
                rstd(2)(g)
                degrees(n)
                rstd(3)(g)
                rstd(1)(n)

            run_steps(nc.gpsimd, step)

        @block.scalar
        def _(act):
            nc.scalar.preload_act_table_set(ACT_SET)
            small = [
                (w0c[:, 0:F], w0.rearrange("d h f -> d (h f)")),
                (a_bc[:, 0, :], a_src.rearrange("h f -> (h f)").partition_broadcast(P)),
                (a_bc[:, 1, :], a_dst.rearrange("h f -> (h f)").partition_broadcast(P)),
                (bias0_bc[:], bias0.partition_broadcast(P)),
                (b2_bc[:], b2.partition_broadcast(P)),
                (gamma_bc[:], gamma.partition_broadcast(P)),
                (beta_bc[:], beta.partition_broadcast(P)),
                (b1_sb[:], b1.rearrange("(t p) f -> p t f", p=P)),
                (w2_in[:], w2),
                (w3_self[:], w_self),
                (w3_neigh[:], w_neigh),
                (mask_in[:], nodemask.rearrange("g (t p) -> (g t) p", p=P)),
                (w1_edge[:], w1[:, F:F + REL, :].rearrange("r d o -> d r o")),
            ]
            for dst, src in small:
                act.dma_start(dst, src).then_inc(s_const, 16)
            for n, r in enumerate(ORDER):
                act.dma_start(w1_sb[:, n, :], w1[r, 0:F, :]).then_inc(s_const, 16)
            act.dma_start(edge_t[:], w_edges.rearrange("r d -> d r"), allow_slow_non_contiguous=True).then_inc(s_rows, 16)
            act.wait_ge(s_setup, 5)
            cuts = ((0, 0, 2), (1, 0, 2), (0, 0, 2), (0, 2, 4), (1, 2, 4), (0, 2, 4), (0, 4, 7), (1, 4, 7))
            for row, (part, lo, hi) in enumerate(cuts):
                act.dma_start(c_rows[row:row + 1, lo * F:hi * F].bitcast(fp32),
                              c_split[0:1, part, lo * F:hi * F].bitcast(fp32)).then_inc(s_rows, 16)

            def scaled(dst, src, scale, func=ACT.Copy):
                for t in range(T):
                    last = nc.scalar.activation(dst[:, t, :], src[:, t, :], func, scale=scale[:, t:t + 1])
                return last

            @of_graph
            def adjacency(g):
                for t in range(T):
                    act.wait_ge(adj_ps, g.th(t + 1, T))
                    if t == 0:
                        if g.has(2):
                            act.wait_ge(g3_ps, g.before(2).all(1))
                        if g.has(2):
                            act.wait_ge(cols_ok, g.before(2).all(2))
                        if g.has(2):
                            act.wait_ge(deg_in, g.before(2).all(3))
                    nc.scalar.activation(adj_tr[g.par][:, t, :], early_t[t % 2][:], ACT.Copy,
                                         accum_out=sums[g.par][:, 0, t:t + 1]).then_inc(adj_sb, 1)

            @of_graph
            def row_sums(g):
                act.wait_ge(s_adj[g.par], g.loaded())
                if g.has(1):
                    act.wait_ge(row_sum, g.before(1).all(1))
                for t in range(T):
                    last = nc.scalar.activation(junk[:, t, :], adj_in[g.par][:, t, :], ACT.Copy,
                                                accum_out=sums[g.par][:, 1, t:t + 1])
                last.then_inc(row_sum, 1)

            @of_graph
            def hidden0(g):
                act.wait_ge(pow0, g.all(1))
                act.wait_ge(cen0, g.all(1))
                if g.has(1):
                    act.wait_ge(h0t_ps, g.before(1).all(1))
                scaled(h0, g0, rstd0).then_inc(h0_ok, 1)

            @of_graph
            def h0_transposed(g):
                act.wait_ge(h0t_ps, g.all(1))
                if g.has(1):
                    act.wait_ge(proj_ps, g.before(1).all(1))
                nc.scalar.copy(h0t[:], early_t[0][:]).then_inc(h0t_sb, 1)

            @of_graph
            def projected(g):
                act.wait_ge(proj_ps, g.all(1))
                if g.has(1):
                    act.wait_ge(val_ok, g.before(1).all(1))
                    act.wait_ge(mean_ps, g.before(1).all(1))
                act.wait_ge(sd_ok, g.all(1))
                nc.scalar.copy(hv[:].rearrange("p (a b) f -> p a b f", a=2),
                               early_a[:, :, 0:272].rearrange("p a (b c) -> p a b c", b=2)[:, :, :, 0:F]
                               ).then_inc(hv_ok, 1)

            @of_graph
            def no_edges(g):
                act.wait_ge(edges, g.all(1))
                if g.has(1):
                    act.wait_ge(pos_used, g.before(1).all(HEADS))
                nc.scalar.mul(nmask[:], mask[:], -1.0).then_inc(nedges, 1)

            @of_graph
            def weights(g):
                act.wait_ge(rel_ok, g.th(1, 2))
                if g.has(1):
                    act.wait_ge(valc_ok, g.before(1).all(1))
                nc.scalar.activation(b12[:, :, :, 0], s_rel[:], ACT.Exp, bias=shift_c[:, 0:1])
                nc.scalar.activation(b12[:, :, :, 1], s_rel[:], ACT.Exp, bias=shift_c[:, 0:1],
                                     scale=SLOPE).then_inc(b_ok, 1)
                act.wait_ge(rel_ok, g.all(2))
                if g.has(1):
                    act.wait_ge(num_ok, g.before(1).all(2))
                nc.scalar.activation(a2[:], d_low[:], ACT.Exp).then_inc(b_ok, 1)

            @of_graph
            def part_hi(g):
                act.wait_ge(val_ok, g.all(1))
                act.wait_ge(valc_ok, g.all(1))
                if g.has(1):
                    act.wait_ge(pos_used, g.before(1).all(HEADS))
                nc.scalar.copy(parts[0][:], val[:]).then_inc(hi_ok, 1)

            @of_graph
            def part_mid(g):
                act.wait_ge(rest_ok, g.all(1))
                nc.scalar.copy(parts[1][:], rest[:]).then_inc(mid_ok, 1)

            @of_graph
            def sums_across(g):
                act.wait_ge(sums_ps, g.all(1))
                if g.has(1):
                    act.wait_ge(hw_ps, g.before(1).all(T))
                nc.scalar.copy(sum_rows[:], bank[3][0:8, :]).then_inc(sums_sb, 1)

            @of_graph
            def hidden1(g):
                act.wait_ge(powl, g.th(1, 3))
                act.wait_ge(cenl, g.th(1, 3))
                if g.has(1):
                    act.wait_ge(h1t_ps, g.before(1).all(3))
                scaled(h1, gl, rstdl).then_inc(hl, 1)

            def operand(k, dst):
                @of_graph
                def piece(g):
                    act.wait_ge(h1t_ps, g.th(k + 1, 3))
                    nc.scalar.copy(dst[:], bank[k]).then_inc(h1t_sb, 1)
                return piece

            @of_graph
            def hidden2(g):
                act.wait_ge(powl, g.th(2, 3))
                act.wait_ge(cenl, g.th(2, 3))
                if g.has(1):
                    act.wait_ge(h2t_ps, g.before(1).all(1))
                scaled(h2, gl, rstdl).then_inc(hl, 1)

            @of_graph
            def h2_transposed(g):
                act.wait_ge(h2t_ps, g.all(1))
                nc.scalar.copy(h2t[:], bank[0]).then_inc(h2t_sb, 1)

            @of_graph
            def conv_in(g):
                act.wait_ge(lin2_ok, g.all(1))
                scaled(y2, lin2, deg_pow[g.par][:, 0, :]).then_inc(y2_ok, 1)

            @of_graph
            def conv_out(g):
                act.wait_ge(ay2_ps, g.all(1))
                nc.scalar.copy(ay2t[:], bank[2]).then_inc(ay2_sb, 1)

            @of_graph
            def conv_relu(g):
                act.wait_ge(back_ps, g.all(1))
                if g.has(1):
                    act.wait_ge(x3_ok, g.before(1).all(1))
                scaled(r2, bank[3].rearrange("p (t f) -> p t f", t=T), scales[g.par][:, 2, :],
                       ACT.Relu).then_inc(r2_ok, 1)

            @of_graph
            def laplace_in(g):
                act.wait_ge(xn_ok, g.all(1))
                scaled(z3, xn, scales[g.par][:, 1, :]).then_inc(z3_ok, 1)

            @of_graph
            def xn_transposed(g):
                act.wait_ge(xnt_ps, g.all(1))
                nc.scalar.copy(xnt[:], bank[0]).then_inc(xnt_sb, 1)

            @of_graph
            def laplace_out(g):
                act.wait_ge(g3_ps, g.all(1))
                nc.scalar.copy(g3t[:], bank[1]).then_inc(g3_sb, 1)

            @of_graph
            def laplace_scaled(g):
                act.wait_ge(p3_ps, g.all(1))
                if g.has(1):
                    act.wait_ge(pre_ok, g.before(1).all(1))
                scaled(p2, bank[3].rearrange("p (t f) -> p t f", t=T), scales[g.par][:, 0, :]
                       ).then_inc(p2_ok, 1)

            @of_graph
            def softplus(g):
                act.wait_ge(pre_ok, g.all(1))
                nc.scalar.activation(mag[:], pre[:], ACT.Abs).then_inc(soft, 1)
                act.wait_ge(soft, g.th(1, 3))
                nc.scalar.activation(ex[:], mag[:], ACT.Exp, scale=-1.0).then_inc(soft, 1)
                act.wait_ge(soft, g.th(2, 3))
                nc.scalar.activation(lg[:], ex[:], ACT.Ln, bias=1.0).then_inc(soft, 1)

            act.wait_ge(s_setup, 4)

            def step(p, g, n):
                adjacency(n)
                sums_across(g)
                operand(0, h1t)(g)
                hidden0(n)
                h0_transposed(n)
                operand(1, aht)(g)
                projected(n)
                weights(n)
                operand(2, atht)(g)
                no_edges(n)
                part_hi(n)
                part_mid(n)
                softplus(p)
                row_sums(n)
                hidden2(g)
                h2_transposed(g)
                conv_in(g)
                conv_out(g)
                conv_relu(g)
                laplace_in(g)
                xn_transposed(g)
                laplace_out(g)
                hidden1(n)
                laplace_scaled(g)

            run_steps(nc.scalar, step)

        @block.vector
        def _(dve):
            V = nc.vector
            V.memset(c_rows[:].bitcast(fp32), 0.0)
            V.memset(shift_c[:], SHIFT)
            V.memset(mean_w[:], 1.0 / N)
            for i in range(2):
                last = V.memset(sum_cols[i][:, :, 6:8].bitcast(fp32), 1.0)
            last.then_inc(s_setup, 1)
            dve.wait_ge(s_const, 16 * CONST_LOADS)
            V.tensor_tensor(wa_tmp[:], a_bc[:], w0c[:, 0:F].unsqueeze(1).broadcast_to([P, 2, F]), ALU.mult
                            ).then_inc(s_setup, 1)
            V.tensor_tensor(w3_sum[:], w3_self[:], w3_neigh[:], ALU.add)
            dve.wait_ge(s_setup, 2)
            V.tensor_reduce(w0c[:, F:F + 2 * HEADS], wa_tmp[:].rearrange("p a (h f) -> p (a h) f", h=HEADS),
                            AX.X, ALU.add)
            dve.wait_ge(s_setup_pe, 1)
            V.tensor_copy(w2_t[:], early_t[0][:, 0:P])
            V.tensor_copy(mask_t[:].rearrange("p g t -> p (g t)"), early_t[0][:, P:P + GRAPHS * T])
            V.tensor_copy(c_row[:].rearrange("p r f -> p (r f)"),
                          early_a[0:1, :, :].rearrange("p a n -> p (a n)")[:, 0:RELS * F]).then_inc(s_setup, 1)
            dve.wait_ge(s_setup, 3)
            c_flat = c_row[:].rearrange("p r f -> p (r f)")
            V.tensor_copy(c_split[:, 0, :], c_flat).then_inc(s_setup, 1)
            dve.wait_ge(s_setup, 4)
            V.tensor_tensor(c_split[:, 1, :], c_flat, c_split[:, 0, :].bitcast(fp32), ALU.subtract
                            ).then_inc(s_setup, 1)

            def norm(src, g, stats, mv, ve, cen, relu, bn, per, k, cen_sig):
                for t in range(T):
                    last = V.bn_stats(stats[:, t, :], src[:, t, :])
                last.then_inc(bn, 1)
                dve.wait_ge(bn, g.th(3 * k + 1, per))
                dve.sem_inc(gate_dve, 1)
                for t in range(T):
                    last = V.bn_aggr(mv[:, t, :], stats[:, t, :])
                last.then_inc(bn, 1)
                dve.wait_ge(bn, g.th(3 * k + 2, per))
                V.tensor_scalar(ve[:], mv[:, :, 1], LN_EPS, None, ALU.add).then_inc(bn, 1)
                for t in range(T):
                    if relu:
                        last = V.tensor_scalar(cen[:, t, :], src[:, t, :], mv[:, t, 0:1], 0.0,
                                               ALU.subtract, ALU.max)
                    else:
                        last = V.tensor_scalar(cen[:, t, :], src[:, t, :], mv[:, t, 0:1], None,
                                               ALU.subtract)
                last.then_inc(cen_sig, 1)

            @of_graph
            def norm0(g):
                dve.wait_ge(s_x[g.par], g.loaded())
                if g.has(1):
                    dve.wait_ge(h0_ok, g.before(1).all(1))
                norm(x_in[g.par], g, st0, mv0, ve0, g0, True, bn0, 3, 0, cen0)

            @of_graph
            def edge_mask(g):
                dve.wait_ge(adj_sb, g.all(T))
                if g.has(1):
                    dve.wait_ge(nedges, g.before(1).all(1))
                if g.has(1):
                    dve.wait_ge(pos_ok, g.before(1).all(HEADS))
                V.tensor_scalar(mask[:], adj_tr[g.par][:], EDGE, None, ALU.is_gt).then_inc(edges, 1)

            @of_graph
            def degrees(g):
                dve.wait_ge(row_sum, g.all(1))
                if g.has(2):
                    dve.wait_ge(p3_ps, g.before(2).all(1))
                if g.has(2):
                    dve.wait_ge(deg_ok, g.before(2).all(1))
                V.tensor_scalar(zero_deg[g.par][:], sums[g.par][:], 0.0, None, ALU.is_equal).then_inc(deg_in, 1)
                V.tensor_scalar(deg[g.par][:, 0, :], sums[g.par][:, 1, :], 1.0, DEG_EPS, ALU.add, ALU.add
                                ).then_inc(deg_in, 1)
                dve.wait_ge(deg_in, g.th(2, 3))
                V.tensor_tensor(deg[g.par][:, 1:3, :], sums[g.par][:], zero_deg[g.par][:], ALU.add
                                ).then_inc(deg_in, 1)
                cols = sum_cols[g.par]
                if g.has(2):
                    dve.wait_ge(sums_ps, g.before(2).all(1))
                for a, o in ((1, 0), (0, 3)):
                    last = V.tensor_copy(cols[:, :, o:o + 2], sums[g.par][:, a, :].unsqueeze(2).broadcast_to([P, T, 2]))
                last.then_inc(cols_ok, 1)
                dve.wait_ge(cols_ok, g.th(1, 2))
                for a, o in ((1, 0), (0, 3)):
                    last = V.tensor_tensor(cols[:, :, o + 2], sums[g.par][:, a, :],
                                           cols[:, :, o].bitcast(fp32), ALU.subtract)
                last.then_inc(cols_ok, 1)

            @of_graph
            def scores(g):
                dve.wait_ge(proj_ps, g.all(1))
                if g.has(1):
                    dve.wait_ge(b_ok, g.before(1).all(2))
                if g.has(1):
                    dve.wait_ge(pos_ok, g.before(1).all(HEADS))
                if g.has(1):
                    dve.wait_ge(dbc_ps, g.before(1).all(HEADS))
                proj = early_a[:, :, 0:272].rearrange("p a (b c) -> p a b c", b=2)
                V.tensor_copy(sd[:].rearrange("p (a b) k h -> p a b (k h)", a=2), proj[:, :, :, F:F + 8]
                              ).then_inc(sd_ok, 1)
                dve.wait_ge(sd_ok, g.all(1))
                V.tensor_reduce(smax_p[:], sd[:, :, 0, :].rearrange("p t h -> p h t"), AX.X, ALU.max
                                ).then_inc(smaxp_ok, 1)
                V.tensor_scalar(neg_s[:], sd[:, :, 0, :], -1.0, None, ALU.mult).then_inc(negs_ok, 1)

            @of_graph
            def node_scales(g):
                dve.wait_ge(deg_out, g.all(1))
                sc, dp, zd = scales[g.par], deg_pow[g.par], zero_deg[g.par]
                V.tensor_tensor(sc[:, 0, :], zd[:, 0, :], dp[:, 1, :], ALU.subtract)
                V.tensor_tensor(sc[:, 1, :], dp[:, 2, :], zd[:, 1, :], ALU.subtract)
                V.tensor_tensor(sc[:, 2, :], dp[:, 0, :],
                                mask_t[:, bass.ts(g.number(), 1), :].rearrange("p g t -> p (g t)"), ALU.mult
                                ).then_inc(deg_ok, 1)

            @of_graph
            def weights(g):
                dve.wait_ge(smax_ok, g.all(1))
                top = smax[:].unsqueeze(1).broadcast_to([P, T, HEADS])
                V.tensor_tensor(s_rel[:], sd[:, :, 0, :], top, ALU.subtract)
                V.tensor_tensor(d_top[:], sd[:, :, 1, :], top, ALU.add).then_inc(rel_ok, 1)
                dve.wait_ge(rel_ok, g.th(1, 2))
                V.tensor_scalar(d_low[:], d_top[:], SLOPE - 1.0, 0.0, ALU.mult, ALU.min).then_inc(rel_ok, 1)
                dve.wait_ge(b_ok, g.th(1, 2))
                if g.has(1):
                    dve.wait_ge(hi_ok, g.before(1).all(1))
                V.tensor_copy(val[:, :, :, HF], b12[:, :, :, 0])
                V.tensor_copy(val[:, :, :, GRP + HF], b12[:, :, :, 1]).then_inc(valc_ok, 1)

            @of_graph
            def part_rest(g):
                dve.wait_ge(hi_ok, g.all(1))
                if g.has(1):
                    dve.wait_ge(mid_ok, g.before(1).all(1))
                V.tensor_tensor(rest[:], val[:], parts[0][:], ALU.subtract).then_inc(rest_ok, 1)

            @of_graph
            def part_lo(g):
                dve.wait_ge(mid_ok, g.all(1))
                if g.has(1):
                    dve.wait_ge(pos_used, g.before(1).all(HEADS))
                V.tensor_tensor(parts[2][:], rest[:], parts[1][:], ALU.subtract).then_inc(lo_ok, 1)

            def head(h):
                @of_graph
                def piece(g):
                    dve.wait_ge(dbc_ps, g.th(h + 1, HEADS))
                    dve.wait_ge(edges, g.all(1))
                    dve.wait_ge(negs_ok, g.all(1))
                    if h >= 2:
                        dve.wait_ge(pos_used, g.th(h - 1, HEADS))
                    elif g.has(1):
                        dve.wait_ge(pos_used, g.before(1).th(h + 3, HEADS))
                    for t in range(T):
                        last = V.scalar_tensor_tensor(pos[h % 2][:, t, :], early_t[(h + 1) % 2][:],
                                                      neg_s[:, t, h:h + 1], mask[:, t, :],
                                                      ALU.is_gt, ALU.mult)
                    last.then_inc(pos_ok, 1)
                return piece

            def pair(g, q):
                dve.wait_ge(pos_used, g.th(2 * q + 2, HEADS))
                dve.wait_ge(b_ok, g.all(2))
                if q == 0:
                    if g.has(1):
                        dve.wait_ge(end0, g.before(1).all(7))
                else:
                    dve.wait_ge(num_ok, g.th(1, 2))
                hs = slice(2 * q, 2 * q + 2)
                acc = [early_a[:, a, 0:4 * VAL].rearrange("p (b h v) -> p b h v", b=2, h=2) for a in range(2)]
                for a in range(2):
                    last = V.tensor_tensor(low[:, 2 * a:2 * a + 2, :, :], acc[a][:, :, :, GRP:VAL],
                                           a2[:, 2 * a:2 * a + 2, hs].unsqueeze(3).broadcast_to([P, 2, 2, GRP]),
                                           ALU.mult)
                last.then_inc(low_ok, 1)
                dve.wait_ge(low_ok, g.th(q + 1, 2))
                for a in range(2):
                    last = V.tensor_tensor(num[:, 2 * a:2 * a + 2, hs, :], acc[a][:, :, :, 0:GRP],
                                           low[:, 2 * a:2 * a + 2, :, :], ALU.subtract)
                last.then_inc(num_ok, 1)

            @of_graph
            def attention(g):
                pair(g, 1)
                dve.wait_ge(num_ok, g.all(2))
                V.tensor_scalar(empty[:], num[:, :, :, HF], 0.0, None, ALU.is_equal).then_inc(end0, 1)
                dve.wait_ge(end0, g.th(1, 7))
                V.tensor_tensor(den[:], num[:, :, :, HF], empty[:], ALU.add).then_inc(end0, 1)
                dve.wait_ge(mean_ps, g.all(1))
                V.tensor_tensor(xe[:].rearrange("p t (h f) -> p t h f", h=HEADS),
                                early_t[1][:, 0:F].rearrange("p (h f) -> p h f", h=HEADS).unsqueeze(1).broadcast_to(
                                    [P, T, HEADS, HF]),
                                empty[:].unsqueeze(3).broadcast_to([P, T, HEADS, HF]), ALU.mult).then_inc(end0, 1)
                dve.wait_ge(end0, g.th(2, 7))
                V.reciprocal(rden[:], den[:]).then_inc(end0, 1)
                dve.wait_ge(xb_ok, g.all(1))
                dve.wait_ge(end0, g.th(3, 7))
                V.tensor_tensor(xf[:], xe[:], xb[g.par][:], ALU.add).then_inc(end0, 1)
                dve.wait_ge(end0, g.th(4, 7))
                V.tensor_tensor(att[:].rearrange("p t (h f) -> p t h f", h=HEADS), num[:, :, :, 0:HF],
                                rden[:].unsqueeze(3).broadcast_to([P, T, HEADS, HF]), ALU.mult).then_inc(end0, 1)
                dve.wait_ge(end0, g.th(6, 7))
                if g.has(2):
                    dve.wait_ge(x1b_ok, g.before(2).all(1))
                V.tensor_tensor(x1[g.par][:], att[:], xf[:], ALU.add).then_inc(end0, 1)

            @of_graph
            def norm1(g):
                dve.wait_ge(end0, g.all(7))
                if g.has(1):
                    dve.wait_ge(xg_ok, g.before(1).all(1))
                norm(x1[g.par], g, stl, mvl, vel, gl, True, bnl, 12, 0, cenl)

            def largest(t):
                @of_graph
                def piece(g):
                    dve.wait_ge(hw_ps, g.th(t + 1, T))
                    V.tensor_reduce(best[:, t, :], late_a[t % 2][:].rearrange("p a n -> p (a n)")[:, 0:RELS * F]
                                    .rearrange("p (r f) -> p f r", f=F), AX.X, ALU.max).then_inc(best_ok, 1)
                return piece

            @of_graph
            def residual1(g):
                dve.wait_ge(best_ok, g.all(T))
                dve.wait_ge(x1b_ok, g.all(1))
                V.tensor_tensor(x2[:], best[:], x1b[:], ALU.add).then_inc(x2_ok, 1)

            @of_graph
            def norm2(g):
                dve.wait_ge(x2_ok, g.all(1))
                dve.wait_ge(hl, g.th(1, 2))
                norm(x2, g, stl, mvl, vel, gl, True, bnl, 12, 1, cenl)

            @of_graph
            def conv(g):
                dve.wait_ge(lin2_ps, g.all(1))
                if g.has(1):
                    dve.wait_ge(y2_ok, g.before(1).all(1))
                V.tensor_tensor(lin2[:], bank[1].rearrange("p (t f) -> p t f", t=T),
                                b2_bc[:].unsqueeze(1).broadcast_to([P, T, F]), ALU.add).then_inc(lin2_ok, 1)

            @of_graph
            def residual2(g):
                dve.wait_ge(r2_ok, g.all(1))
                V.tensor_tensor(x3[:], x2[:], r2[:], ALU.add).then_inc(x3_ok, 1)

            @of_graph
            def norm3(g):
                dve.wait_ge(x3_ok, g.all(1))
                dve.wait_ge(hl, g.th(2, 2))
                norm(x3, g, stl, mvl, vel, gl, True, bnl, 12, 2, cenl)

            @of_graph
            def norm4(g):
                dve.wait_ge(cenl, g.th(3, 3))
                for t in range(T):
                    last = V.bn_stats(stl[:, t, :], gl[:, t, :])
                last.then_inc(bnl, 1)
                dve.wait_ge(bnl, g.th(10, 12))
                dve.sem_inc(gate_dve, 1)
                for t in range(T):
                    last = V.bn_aggr(mv4[:, t, :], stl[:, t, :])
                last.then_inc(bnl, 1)
                dve.wait_ge(bnl, g.th(11, 12))
                V.scalar_tensor_tensor(ve4[:], vel[:], LN_EPS, mv4[:, :, 1], ALU.mult, ALU.add).then_inc(bnl, 1)
                for t in range(T):
                    last = V.scalar_tensor_tensor(xg[:, t, :], gl[:, t, :], mv4[:, t, 0:1], gamma_bc[:],
                                                  ALU.subtract, ALU.mult)
                last.then_inc(xg_ok, 1)

            @of_graph
            def affine(g):
                dve.wait_ge(powl, g.all(3))
                dve.wait_ge(xg_ok, g.all(1))
                if g.has(1):
                    dve.wait_ge(z3_ok, g.before(1).all(1))
                    dve.wait_ge(xnt_ps, g.before(1).all(1))
                for t in range(T):
                    last = V.scalar_tensor_tensor(xn[:, t, :], xg[:, t, :], rstdl[:, t:t + 1], beta_bc[:],
                                                  ALU.mult, ALU.add)
                last.then_inc(xn_ok, 1)

            @of_graph
            def laplace(g):
                dve.wait_ge(p2_ok, g.all(1))
                if g.has(1):
                    dve.wait_ge(s_store, g.before(1).all(16))
                if g.has(1):
                    dve.wait_ge(soft, g.before(1).all(3))
                V.tensor_tensor(pre[:], p2[:], bank[2].rearrange("p (t f) -> p t f", t=T), ALU.add
                                ).then_inc(pre_ok, 1)

            @of_graph
            def softplus(g):
                dve.wait_ge(soft, g.all(3))
                dve.wait_ge(pre_ok, g.all(1))
                V.scalar_tensor_tensor(sp[:], pre[:], 0.0, lg[:], ALU.max, ALU.add).then_inc(sp_ok, 1)
                dve.wait_ge(sp_ok, g.all(1))
                V.tensor_tensor(y_out[:], sp[:], x3[:], ALU.add).then_inc(y_ok, 1)

            def step(p, g, n):
                norm0(n)
                edge_mask(n)
                scores(n)
                head(0)(n)
                weights(n)
                head(1)(n)
                largest(0)(g)
                part_rest(n)
                largest(1)(g)
                part_lo(n)
                largest(2)(g)
                largest(3)(g)
                residual1(g)
                norm2(g)
                softplus(p)
                degrees(n)
                head(2)(n)
                conv(g)
                if n:
                    pair(n, 0)
                head(3)(n)
                residual2(g)
                norm3(g)
                norm4(g)
                affine(g)
                node_scales(n)
                attention(n)
                norm1(n)
                laplace(g)

            run_steps(nc.vector, step)

        @block.tensor
        def _(pe):
            mm, tr = nc.tensor.matmul, nc.tensor.transpose

            pe.wait_ge(s_pool, 2)
            pe.wait_ge(s_const, 16 * CONST_LOADS)
            pe.wait_ge(s_rows, 16)
            tr(early_t[0][:, 0:P], w2_in[:], ident[:])
            tr(early_t[0][:, P:P + GRAPHS * T], mask_in[:], ident[0:GRAPHS * T, 0:GRAPHS * T])
            for n, r in enumerate(ORDER):
                last = mm(early_a[0:1, n // 4, (n % 4) * F:(n % 4 + 1) * F], edge_t[:, r:r + 1], w1_edge[:, r, :],
                          start=True, stop=True)
            last.then_inc(s_setup_pe, 1)
            pe.wait_ge(s_setup, 3)

            @of_graph
            def adjacency(g):
                pe.wait_ge(s_adj[g.par], g.loaded())
                for t in range(T):
                    if t == 0:
                        if g.has(1):
                            pe.wait_ge(pos_ok, g.before(1).th(HEADS, HEADS))
                    elif t == 1:
                        if g.has(1):
                            pe.wait_ge(end0, g.before(1).th(3, 7))
                    else:
                        pe.wait_ge(adj_sb, g.th(t - 1, T))
                    for i in range(T):
                        last = tr(early_t[t % 2][:, i * P:(i + 1) * P], adj_in[g.par][:, i, t * P:(t + 1) * P],
                                  ident[:])
                    last.then_inc(adj_ps, 1)

            @of_graph
            def h0_transposed(g):
                pe.wait_ge(adj_sb, g.th(3, T))
                pe.wait_ge(h0_ok, g.all(1))
                for t in range(T):
                    last = tr(early_t[0][:, t * P:(t + 1) * P], h0[:, t, :], ident[:])
                last.then_inc(h0t_ps, 1)

            @of_graph
            def project(g):
                pe.wait_ge(h0t_sb, g.all(1))
                if g.has(1):
                    pe.wait_ge(num_ok, g.before(1).all(2))
                for t in range(T):
                    last = mm(early_a[:, t // 2, (t % 2) * 136:(t % 2 + 1) * 136], h0t[:, t * P:(t + 1) * P], w0c[:],
                              start=True, stop=True)
                last.then_inc(proj_ps, 1)

            def head(h):
                @of_graph
                def piece(g):
                    if h < 2:
                        spread(g, h + 2)
                    q, hh = h // 2, h % 2
                    if hh == 0:
                        pe.wait_ge(lo_ok, g.all(1))
                        if q == 0:
                            pe.wait_ge(hv_ok, g.all(1))
                            pe.wait_ge(nedges, g.all(1))
                        else:
                            pe.wait_ge(num_ok, g.th(q, 2))
                        for i in range(T):
                            for t in range(T):
                                for n in range(PARTS):
                                    o = (i % 2) * 2 * VAL
                                    mm(early_a[:, i // 2, o:o + 2 * VAL].rearrange("p (h v) -> p h v", h=2)[:, :, GRP:VAL],
                                       nmask[:, t, i * P:(i + 1) * P], parts[n][:, t, 2 * q:2 * q + 2, GRP:VAL],
                                       start=(i % 2 == 0 and t == 0 and n == 0), stop=False, skip_group_check=True)
                    pe.wait_ge(pos_ok, g.th(h + 1, HEADS))
                    for i in range(T):
                        o = ((i % 2) * 2 + hh) * VAL
                        for t in range(T):
                            for n in range(PARTS):
                                last = mm(early_a[:, i // 2, o:o + VAL], pos[h % 2][:, t, i * P:(i + 1) * P],
                                          parts[n][:, t, h, :], start=False,
                                          stop=(i % 2 == 1 and hh == 1 and t == T - 1 and n == PARTS - 1),
                                          skip_group_check=True)
                    last.then_inc(pos_used, 1)
                return piece

            @of_graph
            def spread01(g):
                pe.wait_ge(sd_ok, g.all(1))
                spread(g, 0)
                spread(g, 1)

            def spread(g, h):
                if h == 0:
                    pe.wait_ge(adj_sb, g.all(T))
                elif h == 1:
                    pe.wait_ge(h0t_sb, g.all(1))
                else:
                    pe.wait_ge(pos_ok, g.th(h - 1, HEADS))
                for i in range(T):
                    last = tr(early_t[(h + 1) % 2][:, i * P:(i + 1) * P],
                              sd[:, i, 1, h:h + 1].broadcast_to([P, P]), ident[:])
                last.then_inc(dbc_ps, 1)

            @of_graph
            def finish(g):
                pe.wait_ge(pos_ok, g.th(3, HEADS))
                for t in range(T):
                    last = mm(early_t[1][:, 0:F], mean_w[:], hv[:, t, :], start=(t == 0), stop=(t == T - 1))
                last.then_inc(mean_ps, 1)

            @of_graph
            def norm1(g):
                pe.wait_ge(cols_ok, g.all(2))
                if g.has(1):
                    pe.wait_ge(p2_ok, g.before(1).all(1))
                for t in range(T):
                    last = tr(bank[3][0:8, t * P:(t + 1) * P], sum_cols[g.par][:, t, :].bitcast(fp32), ident[:])
                last.then_inc(sums_ps, 1)
                pe.wait_ge(hl, g.th(1, 2))
                if g.has(1):
                    pe.wait_ge(xnt_sb, g.before(1).all(1))
                for t in range(T):
                    last = tr(bank[0][:, t * P:(t + 1) * P], h1[:, t, :], ident[:])
                last.then_inc(h1t_ps, 1)
                if g.has(1):
                    pe.wait_ge(pre_ok, g.before(1).all(1))
                pe.wait_ge(adj_sb, g.all(T))
                for t in range(T):
                    last = mm(bank[1], h1[:, t, :], adj_tr[g.par][:, t, :], start=(t == 0), stop=(t == T - 1))
                last.then_inc(h1t_ps, 1)

            @of_graph
            def norm1_tr(g):
                for t in range(T):
                    last = mm(bank[2], h1[:, t, :], adj_in[g.par][:, t, :], start=(t == 0), stop=(t == T - 1))
                last.then_inc(h1t_ps, 1)

            @of_graph
            def relations(g):
                pe.wait_ge(s_rows, 16 * 9)
                for t in range(T):
                    if t == 0:
                        pe.wait_ge(h1t_sb, g.th(3, 3))
                        pe.wait_ge(sums_sb, g.all(1))
                    elif t >= 2:
                        pe.wait_ge(best_ok, g.th(t - 1, T))
                    blk = slice(t * P, (t + 1) * P)
                    acc = late_a[t % 2]
                    mm(acc[:, 0, 0:2 * F], aht[:, blk], w1_sb[:, 0:2, :], start=True, stop=False, skip_group_check=True)
                    mm(acc[:, 0, 2 * F:4 * F], atht[:, blk], w1_sb[:, 2:4, :], start=False, stop=False, skip_group_check=True)
                    mm(acc[:, 0, :], sum_rows[:, blk], c_rows[:, 0:4 * F], start=False, stop=True, skip_group_check=True)
                    mm(acc[:, 1, 0:3 * F], h1t[:, blk], w1_sb[:, 4:7, :], start=True, stop=False)
                    mm(acc[:, 1, 0:3 * F], sum_rows[:, blk], c_rows[:, 4 * F:7 * F], start=False, stop=True
                       ).then_inc(hw_ps, 1)

            @of_graph
            def conv(g):
                pe.wait_ge(hl, g.th(2, 2))
                pe.wait_ge(best_ok, g.all(T))
                for t in range(T):
                    last = tr(bank[0][:, t * P:(t + 1) * P], h2[:, t, :], ident[:])
                last.then_inc(h2t_ps, 1)
                pe.wait_ge(h2t_sb, g.all(1))
                for t in range(T):
                    last = mm(bank[1][:, t * F:(t + 1) * F], h2t[:, t * P:(t + 1) * P], w2_t[:], start=True, stop=True)
                last.then_inc(lin2_ps, 1)

            @of_graph
            def conv_product(g):
                pe.wait_ge(y2_ok, g.all(1))
                for t in range(T):
                    mm(bank[2], y2[:, t, :], adj_tr[g.par][:, t, :], start=(t == 0), stop=False, skip_group_check=True)
                for t in range(T):
                    last = mm(bank[2][:, t * P:(t + 1) * P], y2[:, t, :], ident[:], start=False, stop=(t == T - 1),
                              skip_group_check=True)
                last.then_inc(ay2_ps, 1)

            @of_graph
            def back(g):
                pe.wait_ge(ay2_sb, g.all(1))
                for t in range(T):
                    last = tr(bank[3][:, t * P:(t + 1) * P], ay2t[:, t * P:(t + 1) * P], ident[:])
                last.then_inc(back_ps, 1)

            @of_graph
            def norm3(g):
                pe.wait_ge(xn_ok, g.all(1))
                for t in range(T):
                    last = tr(bank[0][:, t * P:(t + 1) * P], xn[:, t, :], ident[:])
                last.then_inc(xnt_ps, 1)
                pe.wait_ge(z3_ok, g.all(1))
                pe.wait_ge(lin2_ok, g.all(1))
                for t in range(T):
                    last = mm(bank[1], z3[:, t, :], adj_tr[g.par][:, t, :], start=(t == 0), stop=(t == T - 1))
                last.then_inc(g3_ps, 1)

            @of_graph
            def laplace(g):
                pe.wait_ge(xnt_sb, g.all(1))
                pe.wait_ge(ay2_sb, g.all(1))
                for t in range(T):
                    mm(bank[2][:, t * F:(t + 1) * F], xnt[:, t * P:(t + 1) * P], w3_sum[:], start=True, stop=True)
                pe.wait_ge(g3_sb, g.all(1))
                pe.wait_ge(r2_ok, g.all(1))
                for t in range(T):
                    last = mm(bank[3][:, t * F:(t + 1) * F], g3t[:, t * P:(t + 1) * P], w3_neigh[:], start=True, stop=True)
                last.then_inc(p3_ps, 1)

            def step(p, g, n):
                adjacency(n)
                norm1(g)
                h0_transposed(n)
                project(n)
                spread01(n)
                norm1_tr(g)
                relations(g)
                head(0)(n)
                head(1)(n)
                conv(g)
                conv_product(g)
                back(g)
                head(2)(n)
                head(3)(n)
                finish(n)
                norm3(g)
                laplace(g)

            run_steps(nc.tensor, step)


_INS = ["x", "adj", "nodemask", "L0_gnn_W", "L0_gnn_a_src", "L0_gnn_a_dst", "L0_gnn_bias", "L1_gnn_W",
        "L1_gnn_W_edges", "L1_gnn_b", "L2_gnn_W", "L2_gnn_b", "L3_gnn_gamma", "L3_gnn_beta",
        "L3_gnn_W_self", "L3_gnn_W_neigh"]
_OUT = ((GRAPHS, N, F), "float32")


def kernel(**inputs):
    import numpy as np
    import concourse.bacc as bacc
    from concourse.bass_utils import run_bass_kernel_spmd as run

    nc = bacc.Bacc("TRN2", target_bir_lowering=False, num_devices=1)
    arrays, args = {}, []
    for name in _INS:
        a = np.ascontiguousarray(inputs[name])
        arrays[f"in_{name}"] = a
        args.append(nc.dram_tensor(f"in_{name}", a.shape, mybir.dt.from_np(a.dtype), kind="ExternalInput").ap())
    shape, dtype = _OUT
    args.append(nc.dram_tensor("out_y", shape, mybir.dt.from_np(np.dtype(dtype)), kind="ExternalOutput").ap())
    graph_kernel(nc, *args)
    return run(nc, [arrays], core_ids=[0]).results[0]["out_y"]
```
